# Optimizing a Trainium2 kernel written in Bass

```python
import numpy as np
import jax
import jax.numpy as jnp

def _softmax(x, axis=-1):
    return jax.nn.softmax(x, axis=axis)

def _gelu(x):
    return jax.nn.gelu(x, approximate=True)

def _silu(x):
    return jax.nn.silu(x)

def _sigmoid(x):
    return jax.nn.sigmoid(x)

def _layernorm(x, axis=-1, eps=1e-05):
    m = jnp.mean(x, axis=axis, keepdims=True)
    v = jnp.var(x, axis=axis, keepdims=True)
    return (x - m) / jnp.sqrt(v + eps)

def _scatter_add(tgt, idx, src, axis=0):
    return tgt.at[idx].add(src)

def _segment_sum(src, seg, n):
    return jax.ops.segment_sum(src, seg, n)
kernel_name = 'mk_dlrm_tower_d1_rec_r8_503080'

def setup_inputs(seed: int=0):
    np.random.seed(seed)
    _w = jnp.asarray

    def _rec_inputs():
        import jax
        import jax.numpy as jnp
        _tk = jax.random.key(seed)
        dense_ctx = jax.random.normal(jax.random.fold_in(_tk, 190), (512, 16), jnp.float32)
        ids = jnp.stack([jax.random.randint(jax.random.fold_in(_tk, 200 + f), (512,), 0, v, jnp.int32) for f, v in enumerate([1000, 12500, 12500, 1000, 12500, 12500, 125000, 12500, 12500, 12500, 1000, 12500, 1250, 1000, 1250, 1250, 12500, 12500, 125000, 1000, 12500, 1250, 1000, 1000, 1250, 12500, 12500, 12500, 1000, 1000, 1250, 1000, 1250, 1000, 1000, 1000, 12500, 1250, 12500, 1000])], axis=1)
        tbl_0 = 0.05 * jax.random.normal(jax.random.fold_in(_tk, 500 + 0), (1000, 64), jnp.float32)
        tbl_1 = 0.05 * jax.random.normal(jax.random.fold_in(_tk, 500 + 1), (12500, 64), jnp.float32)
        tbl_2 = 0.05 * jax.random.normal(jax.random.fold_in(_tk, 500 + 2), (12500, 64), jnp.float32)
        tbl_3 = 0.05 * jax.random.normal(jax.random.fold_in(_tk, 500 + 3), (1000, 64), jnp.float32)
        tbl_4 = 0.05 * jax.random.normal(jax.random.fold_in(_tk, 500 + 4), (12500, 64), jnp.float32)
        tbl_5 = 0.05 * jax.random.normal(jax.random.fold_in(_tk, 500 + 5), (12500, 64), jnp.float32)
        tbl_6 = 0.05 * jax.random.normal(jax.random.fold_in(_tk, 500 + 6), (125000, 64), jnp.float32)
        tbl_7 = 0.05 * jax.random.normal(jax.random.fold_in(_tk, 500 + 7), (12500, 64), jnp.float32)
        tbl_8 = 0.05 * jax.random.normal(jax.random.fold_in(_tk, 500 + 8), (12500, 64), jnp.float32)
        tbl_9 = 0.05 * jax.random.normal(jax.random.fold_in(_tk, 500 + 9), (12500, 64), jnp.float32)
        tbl_10 = 0.05 * jax.random.normal(jax.random.fold_in(_tk, 500 + 10), (1000, 64), jnp.float32)
        tbl_11 = 0.05 * jax.random.normal(jax.random.fold_in(_tk, 500 + 11), (12500, 64), jnp.float32)
        tbl_12 = 0.05 * jax.random.normal(jax.random.fold_in(_tk, 500 + 12), (1250, 64), jnp.float32)
        tbl_13 = 0.05 * jax.random.normal(jax.random.fold_in(_tk, 500 + 13), (1000, 64), jnp.float32)
        tbl_14 = 0.05 * jax.random.normal(jax.random.fold_in(_tk, 500 + 14), (1250, 64), jnp.float32)
        tbl_15 = 0.05 * jax.random.normal(jax.random.fold_in(_tk, 500 + 15), (1250, 64), jnp.float32)
        tbl_16 = 0.05 * jax.random.normal(jax.random.fold_in(_tk, 500 + 16), (12500, 64), jnp.float32)
        tbl_17 = 0.05 * jax.random.normal(jax.random.fold_in(_tk, 500 + 17), (12500, 64), jnp.float32)
        tbl_18 = 0.05 * jax.random.normal(jax.random.fold_in(_tk, 500 + 18), (125000, 64), jnp.float32)
        tbl_19 = 0.05 * jax.random.normal(jax.random.fold_in(_tk, 500 + 19), (1000, 64), jnp.float32)
        tbl_20 = 0.05 * jax.random.normal(jax.random.fold_in(_tk, 500 + 20), (12500, 64), jnp.float32)
        tbl_21 = 0.05 * jax.random.normal(jax.random.fold_in(_tk, 500 + 21), (1250, 64), jnp.float32)
        tbl_22 = 0.05 * jax.random.normal(jax.random.fold_in(_tk, 500 + 22), (1000, 64), jnp.float32)
        tbl_23 = 0.05 * jax.random.normal(jax.random.fold_in(_tk, 500 + 23), (1000, 64), jnp.float32)
        tbl_24 = 0.05 * jax.random.normal(jax.random.fold_in(_tk, 500 + 24), (1250, 64), jnp.float32)
        tbl_25 = 0.05 * jax.random.normal(jax.random.fold_in(_tk, 500 + 25), (12500, 64), jnp.float32)
        tbl_26 = 0.05 * jax.random.normal(jax.random.fold_in(_tk, 500 + 26), (12500, 64), jnp.float32)
        tbl_27 = 0.05 * jax.random.normal(jax.random.fold_in(_tk, 500 + 27), (12500, 64), jnp.float32)
        tbl_28 = 0.05 * jax.random.normal(jax.random.fold_in(_tk, 500 + 28), (1000, 64), jnp.float32)
        tbl_29 = 0.05 * jax.random.normal(jax.random.fold_in(_tk, 500 + 29), (1000, 64), jnp.float32)
        tbl_30 = 0.05 * jax.random.normal(jax.random.fold_in(_tk, 500 + 30), (1250, 64), jnp.float32)
        tbl_31 = 0.05 * jax.random.normal(jax.random.fold_in(_tk, 500 + 31), (1000, 64), jnp.float32)
        tbl_32 = 0.05 * jax.random.normal(jax.random.fold_in(_tk, 500 + 32), (1250, 64), jnp.float32)
        tbl_33 = 0.05 * jax.random.normal(jax.random.fold_in(_tk, 500 + 33), (1000, 64), jnp.float32)
        tbl_34 = 0.05 * jax.random.normal(jax.random.fold_in(_tk, 500 + 34), (1000, 64), jnp.float32)
        tbl_35 = 0.05 * jax.random.normal(jax.random.fold_in(_tk, 500 + 35), (1000, 64), jnp.float32)
        tbl_36 = 0.05 * jax.random.normal(jax.random.fold_in(_tk, 500 + 36), (12500, 64), jnp.float32)
        tbl_37 = 0.05 * jax.random.normal(jax.random.fold_in(_tk, 500 + 37), (1250, 64), jnp.float32)
        tbl_38 = 0.05 * jax.random.normal(jax.random.fold_in(_tk, 500 + 38), (12500, 64), jnp.float32)
        tbl_39 = 0.05 * jax.random.normal(jax.random.fold_in(_tk, 500 + 39), (1000, 64), jnp.float32)
        _rk = jax.random.fold_in(_tk, 7)
        W_top1 = 0.0354441 * jax.random.normal(jax.random.fold_in(_tk, 801), (796, 512), jnp.float32)
        W_top2 = 0.0441942 * jax.random.normal(jax.random.fold_in(_tk, 802), (512, 256), jnp.float32)
        W_top3 = 0.0625 * jax.random.normal(jax.random.fold_in(_tk, 803), (256, 1), jnp.float32)
        b_top1 = jnp.zeros((512,), jnp.float32)
        b_top2 = jnp.zeros((256,), jnp.float32)
        return (dense_ctx, ids, tbl_0, tbl_1, tbl_2, tbl_3, tbl_4, tbl_5, tbl_6, tbl_7, tbl_8, tbl_9, tbl_10, tbl_11, tbl_12, tbl_13, tbl_14, tbl_15, tbl_16, tbl_17, tbl_18, tbl_19, tbl_20, tbl_21, tbl_22, tbl_23, tbl_24, tbl_25, tbl_26, tbl_27, tbl_28, tbl_29, tbl_30, tbl_31, tbl_32, tbl_33, tbl_34, tbl_35, tbl_36, tbl_37, tbl_38, tbl_39, W_top1, b_top1, W_top2, b_top2, W_top3)
    dense_ctx, ids, tbl_0, tbl_1, tbl_2, tbl_3, tbl_4, tbl_5, tbl_6, tbl_7, tbl_8, tbl_9, tbl_10, tbl_11, tbl_12, tbl_13, tbl_14, tbl_15, tbl_16, tbl_17, tbl_18, tbl_19, tbl_20, tbl_21, tbl_22, tbl_23, tbl_24, tbl_25, tbl_26, tbl_27, tbl_28, tbl_29, tbl_30, tbl_31, tbl_32, tbl_33, tbl_34, tbl_35, tbl_36, tbl_37, tbl_38, tbl_39, W_top1, b_top1, W_top2, b_top2, W_top3 = _rec_inputs()

    def _L0_rec_setup():
        import jax, jax.numpy as jnp
        import numpy as np

        def _pair_indices(num_fields):
            i_idx, j_idx = np.triu_indices(num_fields, k=1)
            return (jnp.asarray(i_idx), jnp.asarray(j_idx))
        key = jax.random.key(seed)
        k1, k2 = jax.random.split(key)
        B, F, D = (256, 40, 64)
        P = F * (F - 1) // 2
        x = jax.random.normal(k1, (B, F, D), dtype=jnp.float32)
        W = jax.random.normal(k2, (P, D, D), dtype=jnp.float32) * (1.0 / np.sqrt(D))
        return {'x': x, 'W': W}
    _L0_rec_all = _L0_rec_setup()
    _L0_rec_in = {k: v for k, v in _L0_rec_all.items() if k in ('W',)}
    del _L0_rec_all
    return {'dense_ctx': dense_ctx, 'ids': ids, 'tbl_0': tbl_0, 'tbl_1': tbl_1, 'tbl_2': tbl_2, 'tbl_3': tbl_3, 'tbl_4': tbl_4, 'tbl_5': tbl_5, 'tbl_6': tbl_6, 'tbl_7': tbl_7, 'tbl_8': tbl_8, 'tbl_9': tbl_9, 'tbl_10': tbl_10, 'tbl_11': tbl_11, 'tbl_12': tbl_12, 'tbl_13': tbl_13, 'tbl_14': tbl_14, 'tbl_15': tbl_15, 'tbl_16': tbl_16, 'tbl_17': tbl_17, 'tbl_18': tbl_18, 'tbl_19': tbl_19, 'tbl_20': tbl_20, 'tbl_21': tbl_21, 'tbl_22': tbl_22, 'tbl_23': tbl_23, 'tbl_24': tbl_24, 'tbl_25': tbl_25, 'tbl_26': tbl_26, 'tbl_27': tbl_27, 'tbl_28': tbl_28, 'tbl_29': tbl_29, 'tbl_30': tbl_30, 'tbl_31': tbl_31, 'tbl_32': tbl_32, 'tbl_33': tbl_33, 'tbl_34': tbl_34, 'tbl_35': tbl_35, 'tbl_36': tbl_36, 'tbl_37': tbl_37, 'tbl_38': tbl_38, 'tbl_39': tbl_39, 'W_top1': W_top1, 'b_top1': b_top1, 'W_top2': W_top2, 'b_top2': b_top2, 'W_top3': W_top3, 'L0_rec_W': _L0_rec_in['W']}

def reference(dense_ctx, ids, tbl_0, tbl_1, tbl_2, tbl_3, tbl_4, tbl_5, tbl_6, tbl_7, tbl_8, tbl_9, tbl_10, tbl_11, tbl_12, tbl_13, tbl_14, tbl_15, tbl_16, tbl_17, tbl_18, tbl_19, tbl_20, tbl_21, tbl_22, tbl_23, tbl_24, tbl_25, tbl_26, tbl_27, tbl_28, tbl_29, tbl_30, tbl_31, tbl_32, tbl_33, tbl_34, tbl_35, tbl_36, tbl_37, tbl_38, tbl_39, W_top1, b_top1, W_top2, b_top2, W_top3, L0_rec_W):
    import jax
    import jax.numpy as jnp

    def _L0_rec_ref(x, W):
        import jax, jax.numpy as jnp
        import numpy as np

        def _pair_indices(num_fields):
            i_idx, j_idx = np.triu_indices(num_fields, k=1)
            return (jnp.asarray(i_idx), jnp.asarray(j_idx))
        B, F, D = x.shape
        i_idx, j_idx = _pair_indices(F)
        vi = x[:, i_idx, :]
        vj = x[:, j_idx, :]
        viW = jnp.einsum('bpd,pde->bpe', vi, W)
        out = jnp.einsum('bpe,bpe->bp', viW, vj)
        return out
    e = jnp.stack([tbl_0[ids[:, 0]], tbl_1[ids[:, 1]], tbl_2[ids[:, 2]], tbl_3[ids[:, 3]], tbl_4[ids[:, 4]], tbl_5[ids[:, 5]], tbl_6[ids[:, 6]], tbl_7[ids[:, 7]], tbl_8[ids[:, 8]], tbl_9[ids[:, 9]], tbl_10[ids[:, 10]], tbl_11[ids[:, 11]], tbl_12[ids[:, 12]], tbl_13[ids[:, 13]], tbl_14[ids[:, 14]], tbl_15[ids[:, 15]], tbl_16[ids[:, 16]], tbl_17[ids[:, 17]], tbl_18[ids[:, 18]], tbl_19[ids[:, 19]], tbl_20[ids[:, 20]], tbl_21[ids[:, 21]], tbl_22[ids[:, 22]], tbl_23[ids[:, 23]], tbl_24[ids[:, 24]], tbl_25[ids[:, 25]], tbl_26[ids[:, 26]], tbl_27[ids[:, 27]], tbl_28[ids[:, 28]], tbl_29[ids[:, 29]], tbl_30[ids[:, 30]], tbl_31[ids[:, 31]], tbl_32[ids[:, 32]], tbl_33[ids[:, 33]], tbl_34[ids[:, 34]], tbl_35[ids[:, 35]], tbl_36[ids[:, 36]], tbl_37[ids[:, 37]], tbl_38[ids[:, 38]], tbl_39[ids[:, 39]]], axis=1)
    z = _L0_rec_ref(e, L0_rec_W)
    z = z.reshape(z.shape[0], -1)
    h = jnp.concatenate([z, dense_ctx], axis=1)
    h = jnp.maximum(h @ W_top1 + b_top1, 0.0)
    h = jnp.maximum(h @ W_top2 + b_top2, 0.0)
    y = h @ W_top3
    return y

_drawn_inputs = setup_inputs


def setup_inputs(seed=0):
    import zlib

    import numpy as np

    out = dict(_drawn_inputs(seed))
    spreads = {'b_top1': (0.0, 0.1), 'b_top2': (0.0, 0.1)}
    factors = {}
    for name, (base, spread) in spreads.items():
        noise = np.random.default_rng([zlib.crc32(name.encode()), seed]).standard_normal(out[name].shape)
        drawn = base * np.exp(spread * noise) if base else spread * noise
        out[name] = jnp.asarray(drawn.astype(out[name].dtype))
    for name, factor in factors.items():
        out[name] = (out[name] * factor).astype(out[name].dtype)
    return out
```

```python
from contextlib import ExitStack

import numpy as np

import concourse.bass as bass
from concourse import mybir

F32 = mybir.dt.float32
F32R = mybir.dt.float32r
I32 = mybir.dt.int32
ALU = mybir.AluOpType
ACT = mybir.ActivationFunctionType

P = 128
B = 512
BT = B // P
F = 40
D = 64
NB = F // 2
DENSE = 16
H1, H2 = 512, 256
M1, M2 = H1 // P, H2 // P

CHUNKS = [(k, i) for k in range(NB) for i in range(2 * k + 1)]
NCH = len(CHUNKS)
SLOTS = [(k, i, min(2, 2 * k + 1 - i)) for k in range(NB) for i in range(0, 2 * k + 1, 2)]
NS = len(SLOTS)
FIRST_SLOT = [next(n for n, s in enumerate(SLOTS) if s[0] == k) for k in range(NB)] + [NS]
CHUNK_SLOT = [FIRST_SLOT[k] + i // 2 for k, i in CHUNKS]

PIECE = 8
NP = NCH // PIECE
PIECE_FIRST = [CHUNK_SLOT[q * PIECE] for q in range(NP)]
PIECE_LAST = [CHUNK_SLOT[q * PIECE + PIECE - 1] for q in range(NP)]
POOL_FROM = 26

BATCH = 4
NBATCH = NCH // BATCH
BANK_BATCHES = 16
NZ = -(-NBATCH // BANK_BATCHES)

GR, G2R, RAW, SPL, PR, UR, XR, ZR = 4, 2, 3, 4, 5, 2, 2, 2
EARLY = 8


def z_row(c, half):
    batch, group = divmod(c, BATCH)
    bank, s = divmod(batch, BANK_BATCHES)
    return bank * P + 32 * group + 2 * s + half


DENSE_ROW = (NZ - 1) * P + P - DENSE


def split_slot(kb):
    return FIRST_SLOT[kb] - (6 if kb >= EARLY else 0)


def transpose_slots(kb):
    return [FIRST_SLOT[kb] - (3 - r if kb >= EARLY else 0) for r in range(3)]


def batches_after(n):
    lo, hi = n - 2, n - 2
    if n == NS - 1:
        hi = NS - 1
    return [b for b in range(NBATCH) if lo <= CHUNK_SLOT[b * BATCH + BATCH - 1] <= hi]


def program(nc, ids, w_pair, tables, w1, w2, w3, b1, b2, dense, ident, sel, sel_dense, out):
    with ExitStack() as ctx:
        def sb(name, shape, dt=F32):
            return ctx.enter_context(nc.sbuf_tensor(name, shape, dt))

        def psum(name, shape):
            return ctx.enter_context(nc.psum_tensor(name, shape, F32))

        def sem(name):
            return ctx.enter_context(nc.semaphore(name))

        ids_sb = sb("ids_sb", [P, BT, F], I32)
        gath = sb("gath", [P, GR, BT, 2, D])
        gsplit = sb("gsplit", [P, G2R, BT, 2, 2, D], F32R)
        xs = sb("xs", [P, F, B], F32R)
        xm = sb("xm", [P, 2, B])
        raw = sb("raw", [P, RAW, PIECE * P])
        w_hi = sb("w_hi", [P, SPL, PIECE * P], F32R)
        w_lo = sb("w_lo", [P, SPL, PIECE * P], F32R)
        prod = sb("prod", [P, PR, 2, B])
        z_sb = sb("z_sb", [P, NZ, B])
        w1_sb = sb("w1_sb", [P, NZ, H1])
        w2_sb = sb("w2_sb", [P, M1, H2])
        w3_sb = sb("w3_sb", [P, M2])
        b1_sb = sb("b1_sb", [P, M1])
        b2_sb = sb("b2_sb", [P, M2])
        dense_sb = sb("dense_sb", [DENSE, B])
        ident_sb = sb("ident_sb", [P, P])
        sel_sb = sb("sel_sb", [P, 62])
        seld_sb = sb("seld_sb", [DENSE, 32])
        y_sb = sb("y_sb", [1, B])
        h1_sb = prod[:, 0:2, :, :].rearrange("p a c n -> p (a c) n")
        h2_sb = prod[:, 2, :, :]

        u = psum("u", [P, UR, 2, B])
        xp = psum("xp", [P, XR, B])
        zp = psum("zp", [P, ZR, B])
        h1_ps = u[:, :, :, :].rearrange("p a c n -> p (a c) n")
        h2_ps, y_ps = xp, zp[0:1, 0, :]

        ids_in = sem("ids_in")
        const_in = sem("const_in")
        tower_in = sem("tower_in")
        w_loaded = [sem(f"w_loaded{r}") for r in range(RAW)]
        gathered = [sem(f"gathered{r}") for r in range(GR)]
        g_hi_done = sem("g_hi_done")
        g_lo_done = sem("g_lo_done")
        transposed = sem("transposed")
        x_ready = sem("x_ready")
        w_hi_done = sem("w_hi_done")
        w_lo_dve = sem("w_lo_dve")
        w_lo_pool = sem("w_lo_pool")
        u_filled = sem("u_filled")
        prod_ready = sem("prod_ready")
        summed = sem("summed")
        dense_in_z = sem("dense_in_z")
        z_ready = sem("z_ready")
        h1_mm = sem("h1_mm")
        h1_act = sem("h1_act")
        h1_dve = sem("h1_dve")
        h2_mm = sem("h2_mm")
        h2_act = sem("h2_act")
        h2_dve = sem("h2_dve")
        y_mm = sem("y_mm")
        y_ready = sem("y_ready")
        stored = sem("stored")

        def wait_w_lo(eng, q):
            if q < POOL_FROM:
                eng.wait_ge(w_lo_dve, q + 1)
            else:
                eng.wait_ge(w_lo_pool, q - POOL_FROM + 1)

        def form_w_lo(eng, q, done):
            eng.wait_ge(w_hi_done, q + 1)
            eng.tensor_tensor(w_lo[:, q % SPL, :], raw[:, q % RAW, :],
                              w_hi[:, q % SPL, :].bitcast(F32), ALU.subtract).then_inc(done, 1)

        block = ctx.enter_context(nc.Block())

        @block.sync
        def _(sp):
            sp.dma_start(ids_sb[:, :, :], ids).then_inc(ids_in, 16)
            sp.dma_start(ident_sb[:, :], ident).then_inc(const_in, 16)
            sp.dma_start(sel_sb[:, :], sel).then_inc(const_in, 16)
            for q in range(NP):
                if q >= RAW:
                    wait_w_lo(sp, q - RAW)
                for half in range(2):
                    sp.dma_start(raw[half * D:half * D + D, q % RAW, :],
                                 w_pair[q]).then_inc(w_loaded[q % RAW], 16)
                if q == 5:
                    sp.dma_start(seld_sb[:, :], sel_dense).then_inc(tower_in, 16)
                    sp.dma_start(dense_sb[:, :], dense).then_inc(tower_in, 16)
                    sp.dma_start(w1_sb[:, :, :], w1).then_inc(tower_in, 16)
                    sp.dma_start(w2_sb[:, :, :], w2).then_inc(tower_in, 16)
                    sp.dma_start(w3_sb[:, :], w3).then_inc(tower_in, 16)
                    sp.dma_start(b1_sb[:, :], b1).then_inc(tower_in, 16)
                    sp.dma_start(b2_sb[:, :], b2).then_inc(tower_in, 16)
            sp.wait_ge(y_ready, 1)
            sp.dma_start(out, y_sb[:, :]).then_inc(stored, 16)
            sp.wait_ge(stored, 16)

        @block.gpsimd
        def _(pool):
            pool.wait_ge(ids_in, 16)
            q = POOL_FROM
            for kb in range(NB):
                while q < NP and kb >= GR and PIECE_FIRST[q] <= FIRST_SLOT[kb - GR]:
                    form_w_lo(pool, q, w_lo_pool)
                    q += 1
                if kb >= GR:
                    pool.wait_ge(transposed, 3 * (kb - GR) + 2)
                for half in range(2):
                    f = 2 * kb + half
                    for t in range(BT):
                        pool.indirect_dma_start(
                            gath[:, kb % GR, t, half, :], None, tables[f],
                            bass.IndirectOffsetOnAxis(ap=ids_sb[:, t, f:f + 1], axis=0),
                        ).then_inc(gathered[kb % GR], 16)
            for q in range(q, NP):
                form_w_lo(pool, q, w_lo_pool)

        @block.scalar
        def _(act):
            def split_hi(kb):
                act.wait_ge(gathered[kb % GR], 16 * 2 * BT * (kb // GR + 1))
                if kb >= G2R:
                    act.wait_ge(transposed, 3 * (kb - G2R + 1))
                act.activation(gsplit[:, kb % G2R, :, :, 0, :], gath[:, kb % GR, :, :, :],
                               ACT.Copy).then_inc(g_hi_done, 1)

            def take_transposed(kb, r):
                item = 3 * kb + r
                act.wait_ge(transposed, item + 1)
                if r == 0 and kb >= 2:
                    act.wait_ge(prod_ready, FIRST_SLOT[kb - 1])
                to = xm[:, kb % 2, :] if r == 0 else xs[:, 2 * kb + r - 1, :]
                act.activation(to, xp[:, item % XR, :], ACT.Copy).then_inc(x_ready, 1)

            def round_w(q):
                act.wait_ge(w_loaded[q % RAW], 32 * (q // RAW + 1))
                if q >= SPL:
                    act.wait_ge(u_filled, PIECE_LAST[q - SPL] + 1)
                act.activation(w_hi[:, q % SPL, :], raw[:, q % RAW, :],
                               ACT.Copy).then_inc(w_hi_done, 1)

            def take_z(t):
                act.wait_ge(summed, min(BANK_BATCHES * (t + 1), NBATCH))
                if t == NZ - 1:
                    act.wait_ge(dense_in_z, 1)
                act.activation(z_sb[:, t, :], zp[:, t % ZR, :], ACT.Copy).then_inc(z_ready, 1)

            for q in range(SPL - 1):
                round_w(q)
            q = SPL - 1
            z_taken = 0
            for n in range(NS):
                for kb in range(NB):
                    if split_slot(kb) == n:
                        split_hi(kb)
                for kb in range(NB):
                    for r in range(3):
                        if transpose_slots(kb)[r] == n:
                            take_transposed(kb, r)
                while q < NP and (q < SPL or PIECE_LAST[q - SPL] < n):
                    round_w(q)
                    q += 1
                if z_taken < NZ - 1 and n >= 1 and BANK_BATCHES * (z_taken + 1) - 1 in batches_after(n - 1):
                    take_z(z_taken)
                    z_taken += 1
            take_z(NZ - 1)
            act.wait_ge(tower_in, 16 * 7)
            for m in range(0, M1, 2):
                act.wait_ge(h1_mm, m + 1)
                act.activation(h1_sb[:, m, :], h1_ps[:, m, :], ACT.Relu,
                               bias=b1_sb[:, m:m + 1]).then_inc(h1_act, 1)
            act.wait_ge(h2_mm, 1)
            act.activation(h2_sb[:, 0, :], h2_ps[:, 0, :], ACT.Relu,
                           bias=b2_sb[:, 0:1]).then_inc(h2_act, 1)
            act.wait_ge(y_mm, 1)
            act.activation(y_sb[:, :], y_ps, ACT.Copy).then_inc(y_ready, 1)

        @block.tensor
        def _(pe):
            def transpose_item(kb, r):
                item = 3 * kb + r
                if item == 0:
                    pe.wait_ge(const_in, 32)
                if item >= XR:
                    pe.wait_ge(x_ready, item - XR + 1)
                if r == 0:
                    pe.wait_ge(gathered[kb % GR], 16 * 2 * BT * (kb // GR + 1))
                if r == 1:
                    pe.wait_ge(g_lo_done, kb + 1)
                for t in range(BT):
                    if r == 0:
                        rows = gath[:, kb % GR, t, :, :].rearrange("p a d -> p (a d)")
                    else:
                        rows = gsplit[:, kb % G2R, t, r - 1, :, :].bitcast(F32).rearrange("p a d -> p (a d)")
                    mm = pe.transpose(xp[:, item % XR, t * P:(t + 1) * P], rows, ident_sb[:, :])
                mm.then_inc(transposed, 1)

            def fill(n):
                k, i0, count = SLOTS[n]
                if n >= UR:
                    pe.wait_ge(prod_ready, n - UR + 1)
                if i0 + count == 2 * k + 1:
                    pe.wait_ge(x_ready, 3 * k + 2)
                for a in range(count):
                    i = i0 + a
                    c = k * k + i
                    q, at = divmod(c, PIECE)
                    if at == 0:
                        wait_w_lo(pe, q)
                    for w, first in ((w_hi, True), (w_lo, False)):
                        mm = pe.matmul(u[:, n % UR, a, :], w[:, q % SPL, at * P:(at + 1) * P],
                                       xs[:, i, :], start=first, stop=not first)
                mm.then_inc(u_filled, 1)

            def sum_batch(b):
                bank, s = divmod(b, BANK_BATCHES)
                if s == 0 and bank >= ZR:
                    pe.wait_ge(z_ready, bank - ZR + 1)
                pe.wait_ge(prod_ready, CHUNK_SLOT[b * BATCH + BATCH - 1] + 1)
                last = s == BANK_BATCHES - 1 or b == NBATCH - 1
                for g in range(BATCH):
                    k, i = CHUNKS[b * BATCH + g]
                    n = FIRST_SLOT[k] + i // 2
                    mm = pe.matmul(zp[32 * g:32 * g + 32, bank % ZR, :],
                                   sel_sb[:, 30 - 2 * s:62 - 2 * s], prod[:, n % PR, i % 2, :],
                                   start=s == 0, stop=last and not (b == NBATCH - 1 and g == BATCH - 1))
                mm.then_inc(summed, 1)

            for n in range(NS):
                for kb in range(NB):
                    for r in range(3):
                        if transpose_slots(kb)[r] == n:
                            transpose_item(kb, r)
                fill(n)
                for b in batches_after(n):
                    sum_batch(b)
            pe.wait_ge(tower_in, 16 * 7)
            pe.matmul(zp[96:128, (NZ - 1) % ZR, :], seld_sb[:, :], dense_sb[:, :],
                      start=False, stop=True).then_inc(dense_in_z, 1)

            for t in range(NZ):
                pe.wait_ge(z_ready, t + 1)
                for m in range(M1):
                    mm = pe.matmul(h1_ps[:, m, :], w1_sb[:, t, m * P:(m + 1) * P], z_sb[:, t, :],
                                   start=t == 0, stop=t == NZ - 1)
                    if t == NZ - 1:
                        mm.then_inc(h1_mm, 1)
            for t in range(M1):
                if t % 2 == 0:
                    pe.wait_ge(h1_act, t // 2 + 1)
                else:
                    pe.wait_ge(h1_dve, t // 2 + 1)
                for m in range(M2):
                    mm = pe.matmul(h2_ps[:, m, :], w2_sb[:, t, m * P:(m + 1) * P], h1_sb[:, t, :],
                                   start=t == 0, stop=t == M1 - 1)
                    if t == M1 - 1:
                        mm.then_inc(h2_mm, 1)
            pe.wait_ge(h2_act, 1)
            pe.matmul(y_ps, w3_sb[:, 0:1], h2_sb[:, 0, :], start=True, stop=False)
            pe.wait_ge(h2_dve, 1)
            pe.matmul(y_ps, w3_sb[:, 1:2], h2_sb[:, 1, :], start=False, stop=True).then_inc(y_mm, 1)

        @block.vector
        def _(dve):
            def split_lo(kb):
                dve.wait_ge(g_hi_done, kb + 1)
                g, s = gath[:, kb % GR, :, :, :], gsplit[:, kb % G2R, :, :, :, :]
                dve.tensor_tensor(s[:, :, :, 1, :], g, s[:, :, :, 0, :].bitcast(F32),
                                  ALU.subtract).then_inc(g_lo_done, 1)

            def multiply(n):
                k, i0, count = SLOTS[n]
                dve.wait_ge(u_filled, n + 1)
                if i0 == 0:
                    dve.wait_ge(x_ready, 3 * k + 1)
                if n >= PR:
                    k_old, i_old, count_old = SLOTS[n - PR]
                    dve.wait_ge(summed, (k_old * k_old + i_old + count_old - 1) // BATCH + 1)
                x = xm[:, k % 2, :].unsqueeze(1).broadcast_to([P, count, B])
                dve.tensor_tensor(prod[:, n % PR, 0:count, :], u[:, n % UR, 0:count, :], x,
                                  ALU.mult).then_inc(prod_ready, 1)

            for q in range(SPL - 1):
                form_w_lo(dve, q, w_lo_dve)
            q = SPL - 1
            for n in range(NS):
                for kb in range(NB):
                    if split_slot(kb) == n:
                        split_lo(kb)
                multiply(n)
                while q < POOL_FROM and (q < SPL or PIECE_LAST[q - SPL] < n):
                    form_w_lo(dve, q, w_lo_dve)
                    q += 1
            dve.wait_ge(tower_in, 16 * 7)
            for m in range(1, M1, 2):
                dve.wait_ge(h1_mm, m + 1)
                dve.tensor_scalar(h1_sb[:, m, :], h1_ps[:, m, :], b1_sb[:, m:m + 1], 0.0,
                                  ALU.add, ALU.max).then_inc(h1_dve, 1)
            dve.wait_ge(h2_mm, 2)
            dve.tensor_scalar(h2_sb[:, 1, :], h2_ps[:, 1, :], b2_sb[:, 1:2], 0.0,
                              ALU.add, ALU.max).then_inc(h2_dve, 1)


def pair_weights(w):
    pair = {p: n for n, p in enumerate(zip(*np.triu_indices(F, k=1)))}
    rows = np.array([[pair.get((i, 2 * k + half), -1) for half in range(2)] for k, i in CHUNKS])
    padded = np.concatenate([w, np.zeros((1, D, D), w.dtype)])
    got = padded[rows].reshape(NP, PIECE, 2, D, D).transpose(0, 3, 1, 2, 4)
    return np.ascontiguousarray(got).reshape(NP, D, PIECE * 2 * D)


def top_rows(w):
    rows = np.full(NZ * P, -1)
    pair = {p: n for n, p in enumerate(zip(*np.triu_indices(F, k=1)))}
    for c, (k, i) in enumerate(CHUNKS):
        for half in range(2):
            rows[z_row(c, half)] = pair.get((i, 2 * k + half), -1)
    rows[DENSE_ROW:] = len(pair) + np.arange(DENSE)
    padded = np.concatenate([w, np.zeros((1, w.shape[1]), w.dtype)])
    return tiles(padded[rows])


def tiles(w):
    return np.ascontiguousarray(w.reshape(-1, P, w.shape[1]).transpose(1, 0, 2))


def kernel(**inputs):
    import concourse.bacc as bacc
    from concourse.bass_utils import run_bass_kernel_spmd

    x = {name: np.asarray(a) for name, a in inputs.items()}
    sel = np.zeros((P, 62), np.float32)
    sel[:D, 30] = 1
    sel[D:, 31] = 1
    sel_dense = np.zeros((DENSE, 32), np.float32)
    sel_dense[np.arange(DENSE), 32 - DENSE + np.arange(DENSE)] = 1
    data = {
        "ids": np.ascontiguousarray(x["ids"].reshape(BT, P, F).transpose(1, 0, 2)),
        "w_pair": pair_weights(x["L0_rec_W"]),
        "w_top1": top_rows(x["W_top1"]),
        "w_top2": tiles(x["W_top2"]),
        "w_top3": np.ascontiguousarray(x["W_top3"].reshape(M2, P).T),
        "b_top1": np.ascontiguousarray(x["b_top1"].reshape(M1, P).T),
        "b_top2": np.ascontiguousarray(x["b_top2"].reshape(M2, P).T),
        "dense": np.ascontiguousarray(x["dense_ctx"].T),
        "ident": np.eye(P, dtype=np.float32),
        "sel": sel,
        "sel_dense": sel_dense,
    }
    for f in range(F):
        data[f"tbl_{f}"] = x[f"tbl_{f}"]
    nc = bacc.Bacc("TRN2", target_bir_lowering=False, num_devices=1)
    arrays, aps = {}, {}
    for name, a in data.items():
        arrays[f"in_{name}"] = a
        aps[name] = nc.dram_tensor(f"in_{name}", a.shape, mybir.dt.from_np(a.dtype), kind="ExternalInput").ap()
    out = nc.dram_tensor("y", (B, 1), F32, kind="ExternalOutput").ap()
    program(nc, aps["ids"], [aps["w_pair"][q] for q in range(NP)], [aps[f"tbl_{f}"] for f in range(F)],
            aps["w_top1"], aps["w_top2"], aps["w_top3"], aps["b_top1"], aps["b_top2"], aps["dense"],
            aps["ident"], aps["sel"], aps["sel_dense"], out.rearrange("b o -> o b"))
    return run_bass_kernel_spmd(nc, [arrays], core_ids=[0]).results[0]["y"]
```

```python
from contextlib import ExitStack

import numpy as np

import concourse.bass as bass
from concourse import mybir

F32 = mybir.dt.float32
F32R = mybir.dt.float32r
I32 = mybir.dt.int32
ALU = mybir.AluOpType
ACT = mybir.ActivationFunctionType

P = 128
B = 512
BT = B // P
F = 40
D = 64
NB = F // 2
DENSE = 16
H1, H2 = 512, 256
M1, M2 = H1 // P, H2 // P

CHUNKS = [(k, i) for k in range(NB) for i in range(2 * k + 1)]
NCH = len(CHUNKS)
SLOTS = [(k, i, min(2, 2 * k + 1 - i)) for k in range(NB) for i in range(0, 2 * k + 1, 2)]
NS = len(SLOTS)
FIRST_SLOT = [next(n for n, s in enumerate(SLOTS) if s[0] == k) for k in range(NB)] + [NS]
CHUNK_SLOT = [FIRST_SLOT[k] + i // 2 for k, i in CHUNKS]

PIECE = 8
NP = NCH // PIECE
PIECE_FIRST = [CHUNK_SLOT[q * PIECE] for q in range(NP)]
PIECE_LAST = [CHUNK_SLOT[q * PIECE + PIECE - 1] for q in range(NP)]
POOL_FROM = 10

BATCH = 4
NBATCH = NCH // BATCH
BANK_BATCHES = 16
NZ = -(-NBATCH // BANK_BATCHES)

GR, XR, RAW, SPL, PR, UR = 4, 2, 3, 4, 6, 3
LAG = 3

SMALL = 1000
SMALL_BLOCKS = [0, 1, 4]
GATHERED = [k for k in range(NB) if k not in SMALL_BLOCKS]
SMALL_FIELDS = [2 * k + half for k in SMALL_BLOCKS for half in range(2)]
NOH = len(SMALL_FIELDS)
SMALL_PARTS = [range(0, 1), range(1, 2), range(2, 4), range(4, NOH)]
LOOK_UP_SLOTS = {1 + m: (4 + m // 2, m % 2) for m in range(2 * (NOH - 4))}
TC = -(-SMALL // P)
ITEMS2 = 8
OHR, SSR = 2, 4


def z_row(c, half):
    batch, group = divmod(c, BATCH)
    bank, s = divmod(batch, BANK_BATCHES)
    return bank * P + 32 * group + 2 * s + half


DENSE_ROW = (NZ - 1) * P + P - DENSE


ITEMS = [(k, part) for k in range(NB) for part in ((0, 1, 2) if k in SMALL_BLOCKS else (2,))]


def item_slot(k, part):
    if k < 4:
        return FIRST_SLOT[max(k - 1, 0)]
    return FIRST_SLOT[k] - (3 - part if k in SMALL_BLOCKS else 2)


def lo_slot(k):
    return item_slot(k, 2) + (k > 5)


def stack_slot(k):
    return item_slot(k, 2) + (5 if k >= 8 else 3 if k > 5 else 0)


def item_of(m):
    return ITEMS.index((SMALL_FIELDS[m] // 2, SMALL_FIELDS[m] % 2))


def batches_after(n):
    last = NS - 1 if n == NS - 1 else n - LAG
    return [b for b in range(NBATCH) if n - LAG <= CHUNK_SLOT[b * BATCH + BATCH - 1] <= last]


def pool_steps():
    steps = [(FIRST_SLOT[GATHERED[g - GR]] if g >= GR else -1, 0, ("gather", g, half))
             for g in range(len(GATHERED)) for half in range(2)]
    steps += [(PIECE_LAST[q - SPL] + 1, 1, ("w_lo", q, 0)) for q in range(POOL_FROM, NP)]
    return [what for _, _, what in sorted(steps)]


def program(nc, ids, ids_small, small, row_of, w_pair, tables, w1, w2, w3, b1, b2, dense, ident, sel,
            sel_pair, sel_dense, out):
    with ExitStack() as ctx:
        def sb(name, shape, dt=F32):
            return ctx.enter_context(nc.sbuf_tensor(name, shape, dt))

        def psum(name, shape):
            return ctx.enter_context(nc.psum_tensor(name, shape, F32))

        def sem(name):
            return ctx.enter_context(nc.semaphore(name))

        ids_sb = sb("ids_sb", [P, BT, F], I32)
        gath = sb("gath", [P, GR, BT, 2, D])
        x_hi = sb("x_hi", [P, XR, B], F32R)
        x_lo = sb("x_lo", [P, XR, B], F32R)
        xs = sb("xs", [P, F, B], F32R)
        xm = sb("xm", [P, 2, B])
        row_sb = sb("row_sb", [P, TC])
        raw = sb("raw", [P, RAW, PIECE * P])
        w_hi = sb("w_hi", [P, SPL, PIECE * P], F32R)
        w_lo = sb("w_lo", [P, SPL, PIECE * P], F32R)
        prod = sb("prod", [P, PR, 2, B])
        z_sb = sb("z_sb", [P, NZ, B])
        w1_sb = sb("w1_sb", [P, NZ, H1])
        w2_sb = sb("w2_sb", [P, M1, H2])
        w3_sb = sb("w3_sb", [P, M2])
        b1_sb = sb("b1_sb", [P, M1])
        b2_sb = sb("b2_sb", [P, M2])
        dense_sb = sb("dense_sb", [DENSE, B])
        ident_sb = sb("ident_sb", [P, P])
        sel_sb = sb("sel_sb", [P, 62])
        seld_sb = sb("seld_sb", [DENSE, 32])
        selp_raw = sb("selp_raw", [P, 2, P])
        selp_sb = sb("selp_sb", [P, 2, P], F32R)
        y_sb = sb("y_sb", [1, B])
        h1_sb = prod[:, 0:2, :, :].rearrange("p a c n -> p (a c) n")
        h2_sb = prod[:, 2, :, :]
        small_sb = z_sb[:, :, :].rearrange("p f (c d) -> p f c d", c=TC)
        ids_bc = w1_sb[:, :, :].bitcast(I32)
        one_hot = xs[:, F - 2 * SSR - TC * OHR:F - 2 * SSR, :].rearrange("p (r c) n -> p r c n", r=OHR)
        small_split = xs[:, F - 2 * SSR:F, :].rearrange("p (r a) (c h d) -> p r (a c) h d", r=SSR, h=2, d=D)

        u = psum("u", [P, UR, 2, B])
        xp = psum("xp", [P, B])
        zp = psum("zp", [P, B])
        h1_ps = u[:, 0:2, :, :].rearrange("p a c n -> p (a c) n")

        def item_ps(item):
            return zp if item < ITEMS2 and item % 2 == 1 else xp

        h2_ps, y_ps = u[:, 2, :, :], xp[0:1, :]

        ids_in = sem("ids_in")
        const_in = sem("const_in")
        small_in = [sem(f"small_in{part}") for part in range(len(SMALL_PARTS))]
        sel_pair_done = sem("sel_pair_done")
        small_hi_done = sem("small_hi_done")
        small_lo_done = sem("small_lo_done")
        one_hot_done = sem("one_hot_done")
        tower_in = sem("tower_in")
        w_loaded = [sem(f"w_loaded{r}") for r in range(RAW)]
        gathered = [sem(f"gathered{r}") for r in range(GR)]
        x_hi_done = sem("x_hi_done")
        x_lo_done = sem("x_lo_done")
        stacked = [sem(f"stacked{r}") for r in range(XR)]
        item_done = sem("item_done")
        x_ready = sem("x_ready")
        w_hi_done = sem("w_hi_done")
        w_lo_dve = sem("w_lo_dve")
        w_lo_pool = sem("w_lo_pool")
        u_filled = sem("u_filled")
        prod_ready = sem("prod_ready")
        summed = sem("summed")
        z_ready = sem("z_ready")
        h1_mm = sem("h1_mm")
        h1_act = sem("h1_act")
        h1_dve = sem("h1_dve")
        h2_mm = sem("h2_mm")
        h2_act = sem("h2_act")
        h2_dve = sem("h2_dve")
        y_mm = sem("y_mm")
        y_ready = sem("y_ready")
        stored = sem("stored")

        def wait_w_lo(eng, q):
            if q < POOL_FROM:
                eng.wait_ge(w_lo_dve, q + 1)
            else:
                eng.wait_ge(w_lo_pool, q - POOL_FROM + 1)

        def form_w_lo(eng, q, done):
            eng.wait_ge(w_hi_done, q + 1)
            eng.tensor_tensor(w_lo[:, q % SPL, :], raw[:, q % RAW, :],
                              w_hi[:, q % SPL, :].bitcast(F32), ALU.subtract).then_inc(done, 1)

        block = ctx.enter_context(nc.Block())

        def gather_count(g):
            return 16 * 2 * BT * (g // GR + 1)

        @block.sync
        def _(sp):
            def load_w(q):
                if q >= RAW:
                    wait_w_lo(sp, q - RAW)
                for half in range(2):
                    sp.dma_start(raw[half * D:half * D + D, q % RAW, :],
                                 w_pair[q]).then_inc(w_loaded[q % RAW], 16)

            sp.dma_start(ids_sb[:, :, :], ids).then_inc(ids_in, 16)
            sp.dma_start(row_sb[:, :], row_of).then_inc(small_in[0], 16)
            for part, fields in enumerate(SMALL_PARTS):
                a, b = fields.start, fields.stop
                sp.dma_start(small_sb[:, a:b, :, :], small[:, a:b, :, :]).then_inc(small_in[part], 16)
                sp.dma_start(ids_bc[:, a:b, :], ids_small[:, a:b, :]).then_inc(small_in[part], 16)
                if part == 1:
                    sp.dma_start(selp_raw[:, :, :], sel_pair).then_inc(const_in, 16)
                    sp.dma_start(sel_sb[:, :], sel).then_inc(const_in, 16)
                    sp.dma_start(ident_sb[:, :], ident).then_inc(const_in, 16)
                    load_w(0)
            for q in range(1, NP):
                load_w(q)
                if q == 12:
                    sp.dma_start(seld_sb[:, :], sel_dense).then_inc(tower_in, 16)
                    sp.dma_start(dense_sb[:, :], dense).then_inc(tower_in, 16)
                    sp.wait_ge(one_hot_done, NOH * TC)
                    sp.dma_start(w1_sb[:, :, :], w1).then_inc(tower_in, 16)
                    sp.dma_start(w2_sb[:, :, :], w2).then_inc(tower_in, 16)
                    sp.dma_start(w3_sb[:, :], w3).then_inc(tower_in, 16)
                    sp.dma_start(b1_sb[:, :], b1).then_inc(tower_in, 16)
                    sp.dma_start(b2_sb[:, :], b2).then_inc(tower_in, 16)
            sp.wait_ge(y_ready, 1)
            sp.dma_start(out, y_sb[:, :]).then_inc(stored, 16)
            sp.wait_ge(stored, 16)

        @block.gpsimd
        def _(pool):
            pool.wait_ge(ids_in, 16)
            for what, at, half in pool_steps():
                if what == "w_lo":
                    form_w_lo(pool, at, w_lo_pool)
                    continue
                g, f = at, 2 * GATHERED[at] + half
                if g >= GR:
                    pool.wait_ge(item_done, ITEMS.index((GATHERED[g - GR], 2)) + 1)
                for t in range(BT):
                    pool.indirect_dma_start(
                        gath[:, g % GR, t, half, :], None, tables[f],
                        bass.IndirectOffsetOnAxis(ap=ids_sb[:, t, f:f + 1], axis=0),
                    ).then_inc(gathered[g % GR], 16)

        @block.scalar
        def _(act):
            def round_small(f):
                part = next(n for n, fields in enumerate(SMALL_PARTS) if f in fields)
                act.wait_ge(small_in[part], 48 if part == 0 else 32)
                if f >= SSR:
                    act.wait_ge(item_done, item_of(f - SSR) + 1)
                act.activation(small_split[:, f % SSR, :, 0, :], small_sb[:, f, :, :],
                               ACT.Copy).then_inc(small_hi_done, 1)

            def take_item(item):
                k, part = ITEMS[item]
                act.wait_ge(item_done, item + 1)
                if part < 2:
                    act.activation(xs[:, 2 * k + part, :], item_ps(item)[:, :],
                                   ACT.Copy).then_inc(x_ready, 1)
                    return
                if k in GATHERED:
                    g = GATHERED.index(k)
                    if g >= XR:
                        act.wait_ge(stacked[g % XR], 64 * (g // XR))
                    act.activation(x_hi[:, g % XR, :], item_ps(item)[:, :],
                                   ACT.Copy).then_inc(x_hi_done, 1)
                if k >= 2:
                    act.wait_ge(prod_ready, FIRST_SLOT[k - 1])
                act.activation(xm[:, k % 2, :], item_ps(item)[:, :], ACT.Copy).then_inc(x_ready, 1)

            def stack(k):
                g = GATHERED.index(k)
                act.wait_ge(x_lo_done, g + 1)
                for half in range(2):
                    rows = slice(half * D, half * D + D)
                    for part, x in enumerate((x_hi, x_lo)):
                        act.dma_start(xs[part * D:part * D + D, 2 * k + half, :].bitcast(F32),
                                      x[rows, g % XR, :].bitcast(F32)).then_inc(stacked[g % XR], 16)

            def round_w(q):
                act.wait_ge(w_loaded[q % RAW], 32 * (q // RAW + 1))
                if q >= SPL:
                    act.wait_ge(u_filled, PIECE_LAST[q - SPL] + 1)
                act.activation(w_hi[:, q % SPL, :], raw[:, q % RAW, :],
                               ACT.Copy).then_inc(w_hi_done, 1)

            def take_z(t):
                act.wait_ge(summed, min(BANK_BATCHES * (t + 1), NBATCH))
                act.activation(z_sb[:, t, :], zp[:, :], ACT.Copy).then_inc(z_ready, 1)

            def take_small_item(item):
                take_item(item)
                for m in range(SSR, NOH):
                    if item_of(m - SSR) == item:
                        round_small(m)

            round_small(0)
            round_small(1)
            act.wait_ge(const_in, 48)
            act.activation(selp_sb[:, :, :], selp_raw[:, :, :], ACT.Copy).then_inc(sel_pair_done, 1)
            for f in range(2, min(SSR, NOH)):
                round_small(f)
            round_w(0)
            q = 1
            z_taken = 0
            for n in range(NS):
                if z_taken < NZ - 1 and n >= 1 and BANK_BATCHES * (z_taken + 1) - 1 in batches_after(n - 1):
                    take_z(z_taken)
                    z_taken += 1
                if n == 0:
                    for item in range(3):
                        take_small_item(item)
                while q < NP and (q < min(SPL, 2 + n // 3) or 0 <= q - SPL and PIECE_LAST[q - SPL] < n):
                    round_w(q)
                    q += 1
                for item in range(3, len(ITEMS)):
                    if item_slot(*ITEMS[item]) == n:
                        take_small_item(item)
                for k in GATHERED:
                    if stack_slot(k) == n:
                        stack(k)
            take_z(NZ - 1)
            act.wait_ge(tower_in, 16 * 7)
            for m in range(0, M1, 2):
                act.wait_ge(h1_mm, m + 1)
                act.activation(h1_sb[:, m, :], h1_ps[:, m, :], ACT.Relu,
                               bias=b1_sb[:, m:m + 1]).then_inc(h1_act, 1)
            act.wait_ge(h2_mm, 1)
            act.activation(h2_sb[:, 0, :], h2_ps[:, 0, :], ACT.Relu,
                           bias=b2_sb[:, 0:1]).then_inc(h2_act, 1)
            act.wait_ge(y_mm, 1)
            act.activation(y_sb[:, :], y_ps, ACT.Copy).then_inc(y_ready, 1)

        @block.tensor
        def _(pe):
            def form_item(item):
                k, part = ITEMS[item]
                bank = item_ps(item)
                if item >= ITEMS2:
                    pe.wait_ge(x_ready, item)
                elif item >= 2:
                    pe.wait_ge(x_ready, item - 1)
                if k in GATHERED:
                    g = GATHERED.index(k)
                    if g == 0:
                        pe.wait_ge(const_in, 48)
                    pe.wait_ge(gathered[g % GR], gather_count(g))
                    for t in range(BT):
                        rows = gath[:, g % GR, t, :, :].rearrange("p a d -> p (a d)")
                        mm = pe.transpose(bank[:, t * P:(t + 1) * P], rows, ident_sb[:, :])
                elif part == 2:
                    pe.wait_ge(sel_pair_done, 1)
                    pe.wait_ge(x_ready, item)
                    for half in range(2):
                        mm = pe.matmul(bank[:, :], selp_sb[:, half, :], xs[:, 2 * k + half, :],
                                       start=half == 0, stop=half == 1)
                else:
                    m = SMALL_FIELDS.index(2 * k + part)
                    pe.wait_ge(small_lo_done, m + 1)
                    for c in range(TC):
                        pe.wait_ge(one_hot_done, m * TC + c + 1)
                        mm = pe.matmul(bank[:, :], small_split[:, m % SSR, c, :, :].rearrange("p h d -> p (h d)"),
                                       one_hot[:, m % OHR, c, :], start=c == 0, stop=c == TC - 1)
                mm.then_inc(item_done, 1)

            def fill(n):
                k, i0, count = SLOTS[n]
                if n >= UR:
                    pe.wait_ge(prod_ready, n - UR + 1)
                if i0 + count == 2 * k + 1:
                    if k in GATHERED:
                        g = GATHERED.index(k)
                        pe.wait_ge(stacked[g % XR], 64 * (g // XR + 1))
                    else:
                        pe.wait_ge(x_ready, ITEMS.index((k, 1)) + 1)
                for a in range(count):
                    i = i0 + a
                    c = k * k + i
                    q, at = divmod(c, PIECE)
                    if at == 0:
                        wait_w_lo(pe, q)
                    for w, first in ((w_hi, True), (w_lo, False)):
                        mm = pe.matmul(u[:, n % UR, a, :], w[:, q % SPL, at * P:(at + 1) * P],
                                       xs[:, i, :], start=first, stop=not first)
                mm.then_inc(u_filled, 1)

            def sum_batch(b):
                bank, s = divmod(b, BANK_BATCHES)
                if s == 0 and bank > 0:
                    pe.wait_ge(z_ready, bank)
                if b == 0:
                    pe.wait_ge(x_ready, ITEMS2)
                    pe.wait_ge(const_in, 48)
                pe.wait_ge(prod_ready, CHUNK_SLOT[b * BATCH + BATCH - 1] + 1)
                last = s == BANK_BATCHES - 1 or b == NBATCH - 1
                for g in range(BATCH):
                    k, i = CHUNKS[b * BATCH + g]
                    n = FIRST_SLOT[k] + i // 2
                    mm = pe.matmul(zp[32 * g:32 * g + 32, :],
                                   sel_sb[:, 30 - 2 * s:62 - 2 * s], prod[:, n % PR, i % 2, :],
                                   start=s == 0, stop=last)
                mm.then_inc(summed, 1)
                if bank == NZ - 1 and s == 0:
                    pe.wait_ge(tower_in, 16 * 7)
                    pe.matmul(zp[96:128, :], seld_sb[:, :], dense_sb[:, :], start=False, stop=False)

            for n in range(NS):
                for item in range(len(ITEMS)):
                    if item_slot(*ITEMS[item]) == n:
                        form_item(item)
                fill(n)
                for b in batches_after(n):
                    sum_batch(b)
            for t in range(NZ):
                pe.wait_ge(z_ready, t + 1)
                for m in range(M1):
                    mm = pe.matmul(h1_ps[:, m, :], w1_sb[:, t, m * P:(m + 1) * P], z_sb[:, t, :],
                                   start=t == 0, stop=t == NZ - 1)
                    if t == NZ - 1:
                        mm.then_inc(h1_mm, 1)
            for t in range(M1):
                if t % 2 == 0:
                    pe.wait_ge(h1_act, t // 2 + 1)
                else:
                    pe.wait_ge(h1_dve, t // 2 + 1)
                for m in range(M2):
                    mm = pe.matmul(h2_ps[:, m, :], w2_sb[:, t, m * P:(m + 1) * P], h1_sb[:, t, :],
                                   start=t == 0, stop=t == M1 - 1)
                    if t == M1 - 1:
                        mm.then_inc(h2_mm, 1)
            pe.wait_ge(h2_act, 1)
            pe.matmul(y_ps, w3_sb[:, 0:1], h2_sb[:, 0, :], start=True, stop=False)
            pe.wait_ge(h2_dve, 1)
            pe.matmul(y_ps, w3_sb[:, 1:2], h2_sb[:, 1, :], start=False, stop=True).then_inc(y_mm, 1)

        @block.vector
        def _(dve):
            def form_x_lo(k):
                g = GATHERED.index(k)
                dve.wait_ge(x_hi_done, g + 1)
                dve.wait_ge(x_ready, ITEMS.index((k, 2)) + 1)
                dve.tensor_tensor(x_lo[:, g % XR, :], xm[:, k % 2, :], x_hi[:, g % XR, :].bitcast(F32),
                                  ALU.subtract).then_inc(x_lo_done, 1)

            def look_up(m, part):
                if part == 0:
                    dve.wait_ge(small_hi_done, m + 1)
                    to = small_split[:, m % SSR, :, :, :]
                    dve.tensor_tensor(to[:, :, 1, :], small_sb[:, m, :, :], to[:, :, 0, :].bitcast(F32),
                                      ALU.subtract).then_inc(small_lo_done, 1)
                    if m >= OHR:
                        dve.wait_ge(item_done, item_of(m - OHR) + 1)
                for c in range(part * TC // 2, (part + 1) * TC // 2):
                    dve.tensor_scalar(one_hot[:, m % OHR, c, :], ids_bc[:, m, :], row_sb[:, c:c + 1], None,
                                      ALU.is_equal).then_inc(one_hot_done, 1)

            def multiply(n):
                k, i0, count = SLOTS[n]
                dve.wait_ge(u_filled, n + 1)
                if i0 == 0:
                    dve.wait_ge(x_ready, ITEMS.index((k, 2)) + 1)
                if n >= PR:
                    k_old, i_old, count_old = SLOTS[n - PR]
                    dve.wait_ge(summed, (k_old * k_old + i_old + count_old - 1) // BATCH + 1)
                x = xm[:, k % 2, :].unsqueeze(1).broadcast_to([P, count, B])
                dve.tensor_tensor(prod[:, n % PR, 0:count, :], u[:, n % UR, 0:count, :], x,
                                  ALU.mult).then_inc(prod_ready, 1)

            for m in range(4):
                look_up(m, 0)
                look_up(m, 1)
                if m == 1:
                    form_w_lo(dve, 0, w_lo_dve)
            q = 1
            for n in range(NS):
                while q < POOL_FROM and (q < min(SPL, 2 + n // 3) or 0 <= q - SPL and PIECE_LAST[q - SPL] < n):
                    form_w_lo(dve, q, w_lo_dve)
                    q += 1
                for k in GATHERED:
                    if lo_slot(k) == n:
                        form_x_lo(k)
                multiply(n)
                if n in LOOK_UP_SLOTS:
                    look_up(*LOOK_UP_SLOTS[n])
            dve.wait_ge(tower_in, 16 * 7)
            for m in range(1, M1, 2):
                dve.wait_ge(h1_mm, m + 1)
                dve.tensor_scalar(h1_sb[:, m, :], h1_ps[:, m, :], b1_sb[:, m:m + 1], 0.0,
                                  ALU.add, ALU.max).then_inc(h1_dve, 1)
            dve.wait_ge(h2_mm, 2)
            dve.tensor_scalar(h2_sb[:, 1, :], h2_ps[:, 1, :], b2_sb[:, 1:2], 0.0,
                              ALU.add, ALU.max).then_inc(h2_dve, 1)


def pair_number(order, i, j):
    a, b = sorted((order[i], order[j]))
    return a * F - a * (a + 1) // 2 + b - a - 1, order[i] > order[j]


def pair_weights(w, order):
    got = np.zeros((NCH, 2, D, D), w.dtype)
    for c, (k, i) in enumerate(CHUNKS):
        for half in range(2):
            if i < 2 * k + half:
                n, swapped = pair_number(order, i, 2 * k + half)
                got[c, half] = w[n].T if swapped else w[n]
    got = got.reshape(NP, PIECE, 2, D, D).transpose(0, 3, 1, 2, 4)
    return np.ascontiguousarray(got).reshape(NP, D, PIECE * 2 * D)


def top_rows(w, order):
    got = np.zeros((NZ * P, w.shape[1]), w.dtype)
    for c, (k, i) in enumerate(CHUNKS):
        for half in range(2):
            if i < 2 * k + half:
                got[z_row(c, half)] = w[pair_number(order, i, 2 * k + half)[0]]
    got[DENSE_ROW:] = w[F * (F - 1) // 2:]
    return tiles(got)


def tiles(w):
    return np.ascontiguousarray(w.reshape(-1, P, w.shape[1]).transpose(1, 0, 2))


def kernel(**inputs):
    import concourse.bacc as bacc
    from concourse.bass_utils import run_bass_kernel_spmd

    x = {name: np.asarray(a) for name, a in inputs.items()}
    sel = np.zeros((P, 62), np.float32)
    sel[:D, 30] = 1
    sel[D:, 31] = 1
    sel_dense = np.zeros((DENSE, 32), np.float32)
    sel_dense[np.arange(DENSE), 32 - DENSE + np.arange(DENSE)] = 1
    sel_pair = np.zeros((2, D, 2, 2, D), np.float32)
    for half in range(2):
        sel_pair[:, np.arange(D), half, half, np.arange(D)] = 1
    sizes = [x[f"tbl_{f}"].shape[0] for f in range(F)]
    first = [f for f in range(F) if sizes[f] == SMALL][:NOH]
    rest = iter([f for f in range(F) if f not in first])
    order = [first[SMALL_FIELDS.index(f)] if f in SMALL_FIELDS else next(rest) for f in range(F)]
    ids = x["ids"][:, order]
    small = np.zeros((NOH, TC * P, D), np.float32)
    for n, f in enumerate(first):
        small[n, :SMALL] = x[f"tbl_{f}"]
    data = {
        "ids": np.ascontiguousarray(ids.reshape(BT, P, F).transpose(1, 0, 2)),
        "ids_small": np.ascontiguousarray(ids[:, SMALL_FIELDS].T),
        "small": np.ascontiguousarray(small.reshape(NOH, TC, P, D).transpose(2, 0, 1, 3)),
        "row_of": np.arange(TC * P, dtype=np.float32).reshape(TC, P).T.copy(),
        "w_pair": pair_weights(x["L0_rec_W"], order),
        "w_top1": top_rows(x["W_top1"], order),
        "sel_pair": sel_pair.reshape(P, 2, P),
        "w_top2": tiles(x["W_top2"]),
        "w_top3": np.ascontiguousarray(x["W_top3"].reshape(M2, P).T),
        "b_top1": np.ascontiguousarray(x["b_top1"].reshape(M1, P).T),
        "b_top2": np.ascontiguousarray(x["b_top2"].reshape(M2, P).T),
        "dense": np.ascontiguousarray(x["dense_ctx"].T),
        "ident": np.eye(P, dtype=np.float32),
        "sel": sel,
        "sel_dense": sel_dense,
    }
    for f in order:
        if f not in first:
            data[f"tbl_{f}"] = x[f"tbl_{f}"]
    nc = bacc.Bacc("TRN2", target_bir_lowering=False, num_devices=1)
    arrays, aps = {}, {}
    for name, a in data.items():
        arrays[f"in_{name}"] = a
        aps[name] = nc.dram_tensor(f"in_{name}", a.shape, mybir.dt.from_np(a.dtype), kind="ExternalInput").ap()
    out = nc.dram_tensor("y", (B, 1), F32, kind="ExternalOutput").ap()
    ids_small = aps["ids_small"].unsqueeze(0).broadcast_to([P, NOH, B])
    program(nc, aps["ids"], ids_small, aps["small"], aps["row_of"],
            [aps["w_pair"][q] for q in range(NP)], [aps.get(f"tbl_{f}") for f in order],
            aps["w_top1"], aps["w_top2"], aps["w_top3"], aps["b_top1"], aps["b_top2"], aps["dense"],
            aps["ident"], aps["sel"], aps["sel_pair"], aps["sel_dense"], out.rearrange("b o -> o b"))
    return run_bass_kernel_spmd(nc, [arrays], core_ids=[0]).results[0]["y"]
```

```python
from contextlib import ExitStack

import numpy as np

import concourse.bass as bass
from concourse import mybir

F32 = mybir.dt.float32
F32R = mybir.dt.float32r
I32 = mybir.dt.int32
ALU = mybir.AluOpType
AXIS = mybir.AxisListType
ACT = mybir.ActivationFunctionType

P = 128
B = 512
BT = B // P
F = 40
D = 64
NB = F // 2
DENSE = 16
H1, H2 = 512, 256
M1, M2 = H1 // P, H2 // P

J = range(NB - 4, NB)
JF = 2 * len(J)
NU = P // JF
CHUNKS = [(k, i) for k in range(NB) for i in range(NU if k in J else 0, 2 * k + 1)]
NCH = len(CHUNKS)
BATCH = 4
NBATCH = NCH // BATCH
UNIT_FROM, UNIT_STEP = 48, 2.1


def work_order():
    weights, parts, unit, second = [], [], 0, None
    for b in range(NBATCH):
        chunks = CHUNKS[b * BATCH:b * BATCH + BATCH]
        parts += [("chunk", k, i, len(weights) + n) for n, (k, i) in enumerate(chunks)]
        weights += chunks
        if second:
            parts.append(second)
            second = None
        elif unit < NU and b >= UNIT_FROM + UNIT_STEP * unit:
            parts.append(("unit", unit, 0, len(weights)))
            second = ("unit", unit, 1, len(weights))
            weights += [(k, unit) for k in J]
            unit += 1
    assert unit == NU and not second
    return weights, parts


def make_slots(parts):
    slots = []
    for what, k, i, w in parts:
        last = slots[-1] if slots else None
        if what == "chunk" and last and last[:3] == ("chunk", k, i - 1) and last[3:] == (w - 1, 1):
            slots[-1] = last[:4] + (2,)
        else:
            slots.append((what, k, i, w, 1 if what == "chunk" else 2))
    return slots


WEIGHTS, PARTS = work_order()
SLOTS = make_slots(PARTS)
NS = len(SLOTS)
UNIT_SLOTS = [n for n, s in enumerate(SLOTS) if s[0] == "unit"]
CHUNK_AT = {(k, i + a): (n, a) for n, (what, k, i, _, count) in enumerate(SLOTS) if what == "chunk"
            for a in range(count)}
CHUNK_SLOT = [CHUNK_AT[chunk][0] for chunk in CHUNKS]
FIRST_SLOT = [next(n for n, s in enumerate(SLOTS) if s[:2] == ("chunk", k)) for k in range(NB)] + [NS]

PIECE = 8
NP = len(WEIGHTS) // PIECE
PIECE_FIRST = [min(n for n, s in enumerate(SLOTS) if (s[3] + s[4] - 1) // PIECE >= q) for q in range(NP)]
PIECE_LAST = [max(n for n, s in enumerate(SLOTS) if s[3] // PIECE == q or
                  s[0] == "chunk" and (s[3] + s[4] - 1) // PIECE == q) for q in range(NP)]
LATE_PIECE = 26
ON_DVE = [q for q in range(NP) if q < 10 or q < LATE_PIECE and q % 2 == 1]
ON_POOL = [q for q in range(NP) if q not in ON_DVE]
HI_LEAD, DVE_W_LEAD = 6, 3
LATE_LEAD = 9
GATHER_LEAD, W_LEAD, J_EVERY = 24, 7, 6

BANK_BATCHES = 16
NZR = -(-NBATCH // BANK_BATCHES)
NZ = NZR + 1

GR, XR, RAW, SPL, PR, UR = 4, 2, 3, 4, 7, 3
LAG = 4
REDUCE_LAG = 3
REDUCERS = [("act", "pool"), ("act", "dve"), ("act", "pool"), ("act", "act")]
REDUCER = {(n, tile): REDUCERS[r % len(REDUCERS)][tile] for r, n in enumerate(UNIT_SLOTS) for tile in range(2)}
FOLDS = D.bit_length() - 2

SMALL = 1000
SMALL_BLOCKS = [0, 2]
GATHERED = [k for k in range(NB) if k not in SMALL_BLOCKS]
NG = len(GATHERED) - len(J)
SMALL_FIELDS = [2 * k + half for k in SMALL_BLOCKS for half in range(2)]
NOH = len(SMALL_FIELDS)
SMALL_PARTS = [r for r in (range(0, 1), range(1, 2), range(2, 4), range(4, NOH)) if r]
LOOK_UP_SLOTS = {m: (3 + m // 2, m % 2) for m in range(2 * (NOH - 3))}
TC = -(-SMALL // P)
ITEMS2 = 8
OHR, SSR = 2, 4


def z_row(c, half):
    batch, group = divmod(c, BATCH)
    bank, s = divmod(batch, BANK_BATCHES)
    return bank * P + 32 * group + 2 * s + half


def unit_row(i, j):
    return NZR * P + i * JF + j - 2 * J[0]


DENSE_ROW = (NZR - 1) * P + P - DENSE


ITEMS = [(k, part) for k in range(NB) for part in ((0, 1, 2) if k in SMALL_BLOCKS else (2,))]


def item_slot(k, part):
    if k == 2:
        return FIRST_SLOT[1] + part
    if k < 4:
        return FIRST_SLOT[max(k - 1, 0)]
    return FIRST_SLOT[k] - (3 - part if k in SMALL_BLOCKS else 2)


def lo_slot(k):
    return item_slot(k, 2) + (k > 5)


def stack_slot(k):
    return item_slot(k, 2) + (5 if k >= 8 else 3 if k > 5 else 0)


def hi_slot(q):
    return PIECE_LAST[q - SPL] + 1 if q >= SPL else PIECE_FIRST[q] - HI_LEAD


def item_of(m):
    return ITEMS.index((SMALL_FIELDS[m] // 2, SMALL_FIELDS[m] % 2))


def batches_after(n):
    last = NS - 1 if n == NS - 1 else n - LAG
    return [b for b in range(NBATCH) if n - LAG <= CHUNK_SLOT[b * BATCH + BATCH - 1] <= last]


def reduced_by(engine, n):
    return sum(1 for (m, _), by in REDUCER.items() if by == engine and m <= n)


def pool_steps():
    steps = [(item_slot(GATHERED[g], 2) - GATHER_LEAD, ("gather", GATHERED[g], half))
             for g in range(NG) for half in range(2)]
    steps += [(UNIT_SLOTS[0] - J_EVERY * (2 * len(J) - n), ("gather", J[n // 2], n % 2)) for n in range(2 * len(J))]
    steps += [(PIECE_FIRST[q] - (W_LEAD if q < LATE_PIECE else LATE_LEAD), ("w_lo", q, 0)) for q in ON_POOL]
    steps += [(n + REDUCE_LAG, ("reduce", n, tile)) for (n, tile), by in REDUCER.items() if by == "pool"]
    return [what for _, what in sorted(steps, key=lambda step: step[0])]


def program(nc, ids, ids_small, small, row_of, w_pair, tables, w1, w2, w3, b1, b2, dense, ident, sel,
            sel_pair, sel_dense, out):
    with ExitStack() as ctx:
        def sb(name, shape, dt=F32):
            return ctx.enter_context(nc.sbuf_tensor(name, shape, dt))

        def psum(name, shape):
            return ctx.enter_context(nc.psum_tensor(name, shape, F32))

        def sem(name):
            return ctx.enter_context(nc.semaphore(name))

        ids_sb = sb("ids_sb", [P, BT, F], I32)
        gath = sb("gath", [P, GR, BT, 2, D])
        x_hi = sb("x_hi", [P, XR, B], F32R)
        x_lo = sb("x_lo", [P, XR, B], F32R)
        xs = sb("xs", [P, F, B], F32R)
        xm = sb("xm", [P, 2, B])
        row_sb = sb("row_sb", [P, TC])
        raw = sb("raw", [P, RAW, PIECE * P])
        w_hi = sb("w_hi", [P, SPL, PIECE * P], F32R)
        w_lo = sb("w_lo", [P, SPL, PIECE * P], F32R)
        prod = sb("prod", [P, PR, 2, B])
        z_sb = sb("z_sb", [P, NZ, B])
        w1_sb = sb("w1_sb", [P, NZ, H1])
        w3_sb = sb("w3_sb", [P, M2])
        b1_sb = sb("b1_sb", [P, M1])
        b2_sb = sb("b2_sb", [P, M2])
        dense_sb = sb("dense_sb", [DENSE, B])
        ident_sb = sb("ident_sb", [P, P])
        sel_sb = sb("sel_sb", [P, 62])
        seld_sb = sb("seld_sb", [DENSE, 32])
        selp_raw = sb("selp_raw", [P, 2, P])
        selp_sb = sb("selp_sb", [P, 2, P], F32R)
        zu = sb("zu", [P, BT, P])
        h1_sb = prod[:, 0:2, :, :].rearrange("p a c n -> p (a c) n")
        h2_sb = prod[:, 2, :, :]
        w2_sb = gath[:, 0:2, :, :, :].rearrange("p g t h d -> p (g t h d)").rearrange("p (m n) -> p m n", m=M1)
        j_rows = w1_sb[:, NZ - JF // 2:NZ, :].rearrange("p k (t h d) -> p k t h d", t=BT, h=2)
        y_sb = xm[0:1, 0, :]
        small_sb = z_sb[:, :, :].rearrange("p f (c d) -> p f c d", c=TC)
        ids_bc = w1_sb[:, :, :].bitcast(I32)
        one_hot = xs[:, F - 2 * SSR - TC * OHR:F - 2 * SSR, :].rearrange("p (r c) n -> p r c n", r=OHR)
        small_split = xs[:, F - 2 * SSR:F, :].rearrange("p (r a) (c h d) -> p r (a c) h d", r=SSR, h=2, d=D)

        u = psum("u", [P, UR, 2, B])
        xp = psum("xp", [P, B])
        zp = psum("zp", [P, B])
        h1_ps = u[:, 0:2, :, :].rearrange("p a c n -> p (a c) n")

        def item_ps(item):
            return zp if item < ITEMS2 and item % 2 == 1 else xp

        h2_ps, y_ps = u[:, 2, :, :], xp[0:1, :]

        ids_in = sem("ids_in")
        const_in = sem("const_in")
        small_in = [sem(f"small_in{part}") for part in range(len(SMALL_PARTS))]
        sel_pair_done = sem("sel_pair_done")
        small_hi_done = sem("small_hi_done")
        small_lo_done = sem("small_lo_done")
        one_hot_done = sem("one_hot_done")
        tower_in = sem("tower_in")
        w_rest_in = sem("w_rest_in")
        w_loaded = [sem(f"w_loaded{r}") for r in range(RAW)]
        gathered = [sem(f"gathered{r}") for r in range(GR)]
        j_gathered = sem("j_gathered")
        x_hi_done = sem("x_hi_done")
        x_lo_done = sem("x_lo_done")
        stacked = [sem(f"stacked{r}") for r in range(XR)]
        item_done = sem("item_done")
        x_ready = sem("x_ready")
        w_hi_done = sem("w_hi_done")
        w_lo_dve = sem("w_lo_dve")
        w_lo_pool = sem("w_lo_pool")
        u_filled = sem("u_filled")
        prod_ready = sem("prod_ready")
        summed = sem("summed")
        reduced_act = sem("reduced_act")
        reduced_dve = sem("reduced_dve")
        reduced_pool = sem("reduced_pool")
        fold = sem("fold")
        zu_turned = sem("zu_turned")
        z_ready = sem("z_ready")
        h1_mm = sem("h1_mm")
        h1_act = sem("h1_act")
        h1_dve = sem("h1_dve")
        h2_mm = sem("h2_mm")
        h2_act = sem("h2_act")
        h2_dve = sem("h2_dve")
        y_mm = sem("y_mm")
        y_ready = sem("y_ready")
        stored = sem("stored")

        def wait_w_lo(eng, q):
            if q in ON_DVE:
                eng.wait_ge(w_lo_dve, ON_DVE.index(q) + 1)
            else:
                eng.wait_ge(w_lo_pool, ON_POOL.index(q) + 1)

        def form_w_lo(eng, q, done):
            eng.wait_ge(w_hi_done, q + 1)
            eng.tensor_tensor(w_lo[:, q % SPL, :], raw[:, q % RAW, :],
                              w_hi[:, q % SPL, :].bitcast(F32), ALU.subtract).then_inc(done, 1)

        def wait_reduced(eng, n):
            if reduced_by("act", n):
                eng.wait_ge(reduced_act, reduced_by("act", n))
            if reduced_by("dve", n):
                eng.wait_ge(reduced_dve, reduced_by("dve", n))
            if reduced_by("pool", n):
                eng.wait_ge(reduced_pool, reduced_by("pool", n))

        def wait_prod_used(eng, n):
            what, k, i, _, count = SLOTS[n]
            if what == "unit":
                wait_reduced(eng, n)
            else:
                eng.wait_ge(summed, CHUNKS.index((k, i + count - 1)) // BATCH + 1)

        def wait_gathered(eng, k):
            if k in J:
                eng.wait_ge(j_gathered, 16 * 2 * BT * len(J))
            else:
                g = GATHERED.index(k)
                eng.wait_ge(gathered[g % GR], 16 * 2 * BT * (g // GR + 1))

        block = ctx.enter_context(nc.Block())

        def rows_of(k):
            return j_rows[:, J.index(k)] if k in J else gath[:, GATHERED.index(k) % GR]

        @block.sync
        def _(sp):
            def load_w(q):
                if q >= RAW:
                    wait_w_lo(sp, q - RAW)
                for half in range(2):
                    sp.dma_start(raw[half * D:half * D + D, q % RAW, :],
                                 w_pair[q]).then_inc(w_loaded[q % RAW], 16)

            sp.dma_start(ids_sb[:, :, :], ids).then_inc(ids_in, 16)
            sp.dma_start(row_sb[:, :], row_of).then_inc(small_in[0], 16)
            for part, fields in enumerate(SMALL_PARTS):
                a, b = fields.start, fields.stop
                sp.dma_start(small_sb[:, a:b, :, :], small[:, a:b, :, :]).then_inc(small_in[part], 16)
                sp.dma_start(ids_bc[:, a:b, :], ids_small[:, a:b, :]).then_inc(small_in[part], 16)
                if part == 1:
                    sp.dma_start(selp_raw[:, :, :], sel_pair).then_inc(const_in, 16)
                    sp.dma_start(sel_sb[:, :], sel).then_inc(const_in, 16)
                    sp.dma_start(ident_sb[:, :], ident).then_inc(const_in, 16)
                    load_w(0)
            for q in range(1, NP):
                load_w(q)
                if q == 12:
                    sp.dma_start(seld_sb[:, :], sel_dense).then_inc(tower_in, 16)
                    sp.dma_start(dense_sb[:, :], dense).then_inc(tower_in, 16)
                    sp.wait_ge(one_hot_done, NOH * TC)
                    a = NZ - len(J)
                    sp.dma_start(w1_sb[:, :a, :], w1[:, :a, :]).then_inc(tower_in, 16)
                    sp.dma_start(w3_sb[:, :], w3).then_inc(tower_in, 16)
                    sp.dma_start(b1_sb[:, :], b1).then_inc(tower_in, 16)
                    sp.dma_start(b2_sb[:, :], b2).then_inc(tower_in, 16)
            sp.wait_ge(item_done, len(ITEMS))
            sp.wait_ge(prod_ready, UNIT_SLOTS[-1] + 1)
            sp.dma_start(w1_sb[:, a:, :], w1[:, a:, :]).then_inc(w_rest_in, 16)
            sp.dma_start(w2_sb, w2).then_inc(w_rest_in, 16)
            sp.wait_ge(y_ready, 1)
            sp.dma_start(out, y_sb[:, :]).then_inc(stored, 16)
            sp.wait_ge(stored, 16)

        @block.gpsimd
        def _(pool):
            def reduce(n, tile):
                _, i, half, _, _ = SLOTS[n]
                part = prod[:, n % PR, tile, :].rearrange("p (f d) -> p f d", d=D)
                to = zu[:, 2 * half + tile, i * JF:i * JF + JF].unsqueeze(2)
                folds = FOLDS * (folded[0] + 1)
                folded[0] += 1
                pool.wait_ge(prod_ready, n + 1)
                width = D // 2
                while width:
                    if width < D // 2:
                        pool.wait_ge(fold, folds + 1 - width.bit_length())
                    done = pool.tensor_tensor(part[:, :, :width] if width > 1 else to, part[:, :, :width],
                                              part[:, :, width:2 * width], ALU.add)
                    done.then_inc(fold if width > 1 else reduced_pool, 1)
                    width //= 2

            folded = [0]
            pool.wait_ge(ids_in, 16)
            for what, at, half in pool_steps():
                if what == "reduce":
                    reduce(at, half)
                    continue
                if what == "w_lo":
                    form_w_lo(pool, at, w_lo_pool)
                    continue
                f = 2 * at + half
                g = GATHERED.index(at)
                if at in J:
                    pool.wait_ge(one_hot_done, NOH * TC)
                elif g >= GR:
                    pool.wait_ge(item_done, ITEMS.index((GATHERED[g - GR], 2)) + 1)
                for t in range(BT):
                    pool.indirect_dma_start(
                        rows_of(at)[:, t, half, :], None, tables[f],
                        bass.IndirectOffsetOnAxis(ap=ids_sb[:, t, f:f + 1], axis=0),
                    ).then_inc(j_gathered if at in J else gathered[g % GR], 16)

        @block.scalar
        def _(act):
            def round_small(f):
                part = next(n for n, fields in enumerate(SMALL_PARTS) if f in fields)
                act.wait_ge(small_in[part], 48 if part == 0 else 32)
                if f >= SSR:
                    act.wait_ge(item_done, item_of(f - SSR) + 1)
                act.activation(small_split[:, f % SSR, :, 0, :], small_sb[:, f, :, :],
                               ACT.Copy).then_inc(small_hi_done, 1)

            def take_item(item):
                k, part = ITEMS[item]
                act.wait_ge(item_done, item + 1)
                if part < 2:
                    act.activation(xs[:, 2 * k + part, :], item_ps(item)[:, :],
                                   ACT.Copy).then_inc(x_ready, 1)
                    return
                if k in GATHERED:
                    g = GATHERED.index(k)
                    if g >= XR:
                        act.wait_ge(stacked[g % XR], 64 * (g // XR))
                    act.activation(x_hi[:, g % XR, :], item_ps(item)[:, :],
                                   ACT.Copy).then_inc(x_hi_done, 1)
                if k >= 2:
                    act.wait_ge(prod_ready, FIRST_SLOT[k - 1])
                act.activation(xm[:, k % 2, :], item_ps(item)[:, :], ACT.Copy).then_inc(x_ready, 1)

            def stack(k, part):
                g = GATHERED.index(k)
                if part == 0:
                    act.wait_ge(x_hi_done, g + 1)
                else:
                    act.wait_ge(x_lo_done, g + 1)
                for half in range(2):
                    act.dma_start(xs[part * D:part * D + D, 2 * k + half, :].bitcast(F32),
                                  (x_hi, x_lo)[part][half * D:half * D + D, g % XR, :].bitcast(F32)
                                  ).then_inc(stacked[g % XR], 16)

            def round_w(q):
                act.wait_ge(w_loaded[q % RAW], 32 * (q // RAW + 1))
                if q >= SPL:
                    act.wait_ge(u_filled, PIECE_LAST[q - SPL] + 1)
                act.activation(w_hi[:, q % SPL, :], raw[:, q % RAW, :],
                               ACT.Copy).then_inc(w_hi_done, 1)

            def take_z(t):
                act.wait_ge(summed, min(BANK_BATCHES * (t + 1), NBATCH))
                act.activation(z_sb[:, t, :], zp[:, :], ACT.Copy).then_inc(z_ready, 1)

            def reduce(n, tile):
                _, i, half, _, _ = SLOTS[n]
                act.wait_ge(prod_ready, n + 1)
                for f in range(JF):
                    part = prod[:, n % PR, tile, f * D:f * D + D]
                    total = act.activation(part, part, ACT.Copy,
                                           accum_out=zu[:, 2 * half + tile, i * JF + f:i * JF + f + 1])
                total.then_inc(reduced_act, 1)

            def take_small_item(item):
                take_item(item)
                for m in range(SSR, NOH):
                    if item_of(m - SSR) == item:
                        round_small(m)

            round_small(0)
            round_small(1)
            act.wait_ge(const_in, 48)
            act.activation(selp_sb[:, :, :], selp_raw[:, :, :], ACT.Copy).then_inc(sel_pair_done, 1)
            for f in range(2, min(SSR, NOH)):
                round_small(f)
            round_w(0)
            q = 1
            z_taken = 0
            for n in range(NS):
                if z_taken < NZR - 1 and n >= 1 and BANK_BATCHES * (z_taken + 1) - 1 in batches_after(n - 1):
                    take_z(z_taken)
                    z_taken += 1
                for tile in range(2):
                    if REDUCER.get((n - REDUCE_LAG, tile)) == "act":
                        reduce(n - REDUCE_LAG, tile)
                if n == 0:
                    for item in range(3):
                        take_small_item(item)
                while q < NP and hi_slot(q) <= n:
                    round_w(q)
                    q += 1
                for item in range(3, len(ITEMS)):
                    if item_slot(*ITEMS[item]) == n:
                        take_small_item(item)
                for k in GATHERED:
                    if item_slot(k, 2) == n:
                        stack(k, 0)
                for k in GATHERED:
                    if stack_slot(k) == n:
                        stack(k, 1)
            for t in range(z_taken, NZR):
                take_z(t)
            act.wait_ge(zu_turned, 1)
            act.activation(z_sb[:, NZR, :], xp[:, :], ACT.Copy).then_inc(z_ready, 1)
            act.wait_ge(tower_in, 16 * 6)
            for m in range(0, M1, 2):
                act.wait_ge(h1_mm, m + 1)
                act.activation(h1_sb[:, m, :], h1_ps[:, m, :], ACT.Relu,
                               bias=b1_sb[:, m:m + 1]).then_inc(h1_act, 1)
            act.wait_ge(h2_mm, 1)
            act.activation(h2_sb[:, 0, :], h2_ps[:, 0, :], ACT.Relu,
                           bias=b2_sb[:, 0:1]).then_inc(h2_act, 1)
            act.wait_ge(y_mm, 1)
            act.activation(y_sb[:, :], y_ps, ACT.Copy).then_inc(y_ready, 1)

        @block.tensor
        def _(pe):
            def form_item(item):
                k, part = ITEMS[item]
                bank = item_ps(item)
                if item >= ITEMS2:
                    pe.wait_ge(x_ready, item)
                elif item >= 2:
                    pe.wait_ge(x_ready, item - 1)
                if k in GATHERED:
                    g = GATHERED.index(k)
                    if g == 0:
                        pe.wait_ge(const_in, 48)
                    wait_gathered(pe, k)
                    for t in range(BT):
                        rows = rows_of(k)[:, t, :, :].rearrange("p a d -> p (a d)")
                        mm = pe.transpose(bank[:, t * P:(t + 1) * P], rows, ident_sb[:, :])
                elif part == 2:
                    pe.wait_ge(sel_pair_done, 1)
                    pe.wait_ge(x_ready, item)
                    for half in range(2):
                        mm = pe.matmul(bank[:, :], selp_sb[:, half, :], xs[:, 2 * k + half, :],
                                       start=half == 0, stop=half == 1)
                else:
                    m = SMALL_FIELDS.index(2 * k + part)
                    pe.wait_ge(small_lo_done, m + 1)
                    for c in range(TC):
                        pe.wait_ge(one_hot_done, m * TC + c + 1)
                        mm = pe.matmul(bank[:, :], small_split[:, m % SSR, c, :, :].rearrange("p h d -> p (h d)"),
                                       one_hot[:, m % OHR, c, :], start=c == 0, stop=c == TC - 1)
                mm.then_inc(item_done, 1)

            def fill(n):
                what, k, i0, w0, count = SLOTS[n]
                if n >= UR:
                    pe.wait_ge(prod_ready, n - UR + 1)
                if what == "unit":
                    i, half = k, i0
                    q, at = divmod(w0, PIECE)
                    if half == 0:
                        wait_w_lo(pe, q)
                    for tile in range(2):
                        t = 2 * half + tile
                        for w, first in ((w_hi, True), (w_lo, False)):
                            mm = pe.matmul(u[:, n % UR, tile, :], xs[:, i, t * P:t * P + P],
                                           w[:, q % SPL, at * P:(at + len(J)) * P], start=first, stop=not first)
                    mm.then_inc(u_filled, 1)
                    return
                if i0 + count == 2 * k + 1:
                    if k in GATHERED:
                        g = GATHERED.index(k)
                        pe.wait_ge(stacked[g % XR], 64 * (g // XR + 1))
                    else:
                        pe.wait_ge(x_ready, ITEMS.index((k, 1)) + 1)
                for a in range(count):
                    i = i0 + a
                    q, at = divmod(w0 + a, PIECE)
                    if at == 0:
                        wait_w_lo(pe, q)
                    for w, first in ((w_hi, True), (w_lo, False)):
                        mm = pe.matmul(u[:, n % UR, a, :], w[:, q % SPL, at * P:(at + 1) * P],
                                       xs[:, i, :], start=first, stop=not first)
                mm.then_inc(u_filled, 1)

            def sum_batch(b):
                bank, s = divmod(b, BANK_BATCHES)
                if s == 0 and bank > 0:
                    pe.wait_ge(z_ready, bank)
                if b == 0:
                    pe.wait_ge(x_ready, ITEMS2)
                    pe.wait_ge(const_in, 48)
                pe.wait_ge(prod_ready, CHUNK_SLOT[b * BATCH + BATCH - 1] + 1)
                last = s == BANK_BATCHES - 1 or b == NBATCH - 1
                for g in range(BATCH):
                    k, i = CHUNKS[b * BATCH + g]
                    n, at = CHUNK_AT[k, i]
                    mm = pe.matmul(zp[32 * g:32 * g + 32, :],
                                   sel_sb[:, 30 - 2 * s:62 - 2 * s], prod[:, n % PR, at, :],
                                   start=s == 0, stop=last)
                mm.then_inc(summed, 1)
                if bank == NZR - 1 and s == 0:
                    pe.wait_ge(tower_in, 16 * 6)
                    pe.matmul(zp[96:128, :], seld_sb[:, :], dense_sb[:, :], start=False, stop=False)

            for n in range(NS):
                for item in range(len(ITEMS)):
                    if item_slot(*ITEMS[item]) == n:
                        form_item(item)
                fill(n)
                for b in batches_after(n):
                    sum_batch(b)
            for t in range(NZ):
                pe.wait_ge(z_ready, t + 1)
                if t == NZ - len(J):
                    pe.wait_ge(w_rest_in, 32)
                for m in range(M1):
                    mm = pe.matmul(h1_ps[:, m, :], w1_sb[:, t, m * P:(m + 1) * P], z_sb[:, t, :],
                                   start=t == 0, stop=t == NZ - 1)
                    if t == NZ - 1:
                        mm.then_inc(h1_mm, 1)
                if t == 0:
                    wait_reduced(pe, NS - 1)
                    pe.wait_ge(x_ready, len(ITEMS))
                    for tile in range(BT):
                        mm = pe.transpose(xp[:, tile * P:tile * P + P], zu[:, tile, :], ident_sb[:, :])
                    mm.then_inc(zu_turned, 1)
            for t in range(M1):
                if t % 2 == 0:
                    pe.wait_ge(h1_act, t // 2 + 1)
                else:
                    pe.wait_ge(h1_dve, t // 2 + 1)
                for m in range(M2):
                    mm = pe.matmul(h2_ps[:, m, :], w2_sb[:, t, m * P:(m + 1) * P], h1_sb[:, t, :],
                                   start=t == 0, stop=t == M1 - 1)
                    if t == M1 - 1:
                        mm.then_inc(h2_mm, 1)
            pe.wait_ge(h2_act, 1)
            pe.matmul(y_ps, w3_sb[:, 0:1], h2_sb[:, 0, :], start=True, stop=False)
            pe.wait_ge(h2_dve, 1)
            pe.matmul(y_ps, w3_sb[:, 1:2], h2_sb[:, 1, :], start=False, stop=True).then_inc(y_mm, 1)

        @block.vector
        def _(dve):
            def form_x_lo(k):
                g = GATHERED.index(k)
                dve.wait_ge(x_hi_done, g + 1)
                dve.wait_ge(x_ready, ITEMS.index((k, 2)) + 1)
                dve.tensor_tensor(x_lo[:, g % XR, :], xm[:, k % 2, :], x_hi[:, g % XR, :].bitcast(F32),
                                  ALU.subtract).then_inc(x_lo_done, 1)

            def look_up(m, part):
                if part == 0:
                    dve.wait_ge(small_hi_done, m + 1)
                    to = small_split[:, m % SSR, :, :, :]
                    dve.tensor_tensor(to[:, :, 1, :], small_sb[:, m, :, :], to[:, :, 0, :].bitcast(F32),
                                      ALU.subtract).then_inc(small_lo_done, 1)
                    if m >= OHR:
                        dve.wait_ge(item_done, item_of(m - OHR) + 1)
                for c in range(part * TC // 2, (part + 1) * TC // 2):
                    dve.tensor_scalar(one_hot[:, m % OHR, c, :], ids_bc[:, m, :], row_sb[:, c:c + 1], None,
                                      ALU.is_equal).then_inc(one_hot_done, 1)

            def multiply(n):
                what, k, i0, _, count = SLOTS[n]
                dve.wait_ge(u_filled, n + 1)
                if n >= PR:
                    wait_prod_used(dve, n - PR)
                if what == "unit":
                    if n == UNIT_SLOTS[0]:
                        wait_gathered(dve, J[0])
                    rows = j_rows[:, :, 2 * i0:2 * i0 + 2, :, :].rearrange("p k t h d -> p t k (h d)")
                    dve.tensor_tensor(prod[:, n % PR, :, :].rearrange("p t (k f) -> p t k f", k=len(J)),
                                      u[:, n % UR, :, :].rearrange("p t (k f) -> p t k f", k=len(J)),
                                      rows, ALU.mult).then_inc(prod_ready, 1)
                    return
                if n == FIRST_SLOT[k]:
                    dve.wait_ge(x_ready, ITEMS.index((k, 2)) + 1)
                x = xm[:, k % 2, :].unsqueeze(1).broadcast_to([P, count, B])
                dve.tensor_tensor(prod[:, n % PR, 0:count, :], u[:, n % UR, 0:count, :], x,
                                  ALU.mult).then_inc(prod_ready, 1)

            def reduce(n, tile):
                _, i, half, _, _ = SLOTS[n]
                dve.wait_ge(prod_ready, n + 1)
                dve.tensor_reduce(zu[:, 2 * half + tile, i * JF:i * JF + JF],
                                  prod[:, n % PR, tile, :].rearrange("p (f d) -> p f d", d=D),
                                  AXIS.X, ALU.add).then_inc(reduced_dve, 1)

            for m in range(3):
                look_up(m, 0)
                if m == 2:
                    form_x_lo(1)
                look_up(m, 1)
                if m == 1:
                    form_w_lo(dve, 0, w_lo_dve)
            for n in range(NS):
                for q in ON_DVE[1:]:
                    if max(hi_slot(q) + 1, PIECE_FIRST[q] - DVE_W_LEAD, 0) == n:
                        form_w_lo(dve, q, w_lo_dve)
                for k in GATHERED[1:]:
                    if lo_slot(k) == n:
                        form_x_lo(k)
                multiply(n)
                for tile in range(2):
                    if REDUCER.get((n - 1, tile)) == "dve":
                        reduce(n - 1, tile)
                if n in LOOK_UP_SLOTS:
                    look_up(*LOOK_UP_SLOTS[n])
            dve.wait_ge(tower_in, 16 * 6)
            for m in range(1, M1, 2):
                dve.wait_ge(h1_mm, m + 1)
                dve.tensor_scalar(h1_sb[:, m, :], h1_ps[:, m, :], b1_sb[:, m:m + 1], 0.0,
                                  ALU.add, ALU.max).then_inc(h1_dve, 1)
            dve.wait_ge(h2_mm, 2)
            dve.tensor_scalar(h2_sb[:, 1, :], h2_ps[:, 1, :], b2_sb[:, 1:2], 0.0,
                              ALU.add, ALU.max).then_inc(h2_dve, 1)


def pair_number(order, i, j):
    a, b = sorted((order[i], order[j]))
    return a * F - a * (a + 1) // 2 + b - a - 1, order[i] > order[j]


def pair_weights(w, order):
    got = np.zeros((len(WEIGHTS), 2, D, D), w.dtype)
    for c, (k, i) in enumerate(WEIGHTS):
        for half in range(2):
            if i < 2 * k + half:
                n, swapped = pair_number(order, i, 2 * k + half)
                got[c, half] = w[n].T if swapped else w[n]
    got = got.reshape(NP, PIECE, 2, D, D).transpose(0, 3, 1, 2, 4)
    return np.ascontiguousarray(got).reshape(NP, D, PIECE * 2 * D)


def top_rows(w, order):
    got = np.zeros((NZ * P, w.shape[1]), w.dtype)
    for c, (k, i) in enumerate(CHUNKS):
        for half in range(2):
            if i < 2 * k + half:
                got[z_row(c, half)] = w[pair_number(order, i, 2 * k + half)[0]]
    for i in range(NU):
        for j in range(2 * J[0], F):
            got[unit_row(i, j)] = w[pair_number(order, i, j)[0]]
    got[DENSE_ROW:DENSE_ROW + DENSE] = w[F * (F - 1) // 2:]
    return tiles(got)


def tiles(w):
    return np.ascontiguousarray(w.reshape(-1, P, w.shape[1]).transpose(1, 0, 2))


def kernel(**inputs):
    import concourse.bacc as bacc
    from concourse.bass_utils import run_bass_kernel_spmd

    x = {name: np.asarray(a) for name, a in inputs.items()}
    sel = np.zeros((P, 62), np.float32)
    sel[:D, 30] = 1
    sel[D:, 31] = 1
    sel_dense = np.zeros((DENSE, 32), np.float32)
    sel_dense[np.arange(DENSE), 32 - DENSE + np.arange(DENSE)] = 1
    sel_pair = np.zeros((2, D, 2, 2, D), np.float32)
    for half in range(2):
        sel_pair[:, np.arange(D), half, half, np.arange(D)] = 1
    sizes = [x[f"tbl_{f}"].shape[0] for f in range(F)]
    first = [f for f in range(F) if sizes[f] == SMALL][:NOH]
    rest = iter([f for f in range(F) if f not in first])
    order = [first[SMALL_FIELDS.index(f)] if f in SMALL_FIELDS else next(rest) for f in range(F)]
    ids = x["ids"][:, order]
    small = np.zeros((NOH, TC * P, D), np.float32)
    for n, f in enumerate(first):
        small[n, :SMALL] = x[f"tbl_{f}"]
    data = {
        "ids": np.ascontiguousarray(ids.reshape(BT, P, F).transpose(1, 0, 2)),
        "ids_small": np.ascontiguousarray(ids[:, SMALL_FIELDS].T),
        "small": np.ascontiguousarray(small.reshape(NOH, TC, P, D).transpose(2, 0, 1, 3)),
        "row_of": np.arange(TC * P, dtype=np.float32).reshape(TC, P).T.copy(),
        "w_pair": pair_weights(x["L0_rec_W"], order),
        "w_top1": top_rows(x["W_top1"], order),
        "sel_pair": sel_pair.reshape(P, 2, P),
        "w_top2": tiles(x["W_top2"]),
        "w_top3": np.ascontiguousarray(x["W_top3"].reshape(M2, P).T),
        "b_top1": np.ascontiguousarray(x["b_top1"].reshape(M1, P).T),
        "b_top2": np.ascontiguousarray(x["b_top2"].reshape(M2, P).T),
        "dense": np.ascontiguousarray(x["dense_ctx"].T),
        "ident": np.eye(P, dtype=np.float32),
        "sel": sel,
        "sel_dense": sel_dense,
    }
    for f in order:
        if f not in first:
            data[f"tbl_{f}"] = x[f"tbl_{f}"]
    nc = bacc.Bacc("TRN2", target_bir_lowering=False, num_devices=1)
    arrays, aps = {}, {}
    for name, a in data.items():
        arrays[f"in_{name}"] = a
        aps[name] = nc.dram_tensor(f"in_{name}", a.shape, mybir.dt.from_np(a.dtype), kind="ExternalInput").ap()
    out = nc.dram_tensor("y", (B, 1), F32, kind="ExternalOutput").ap()
    ids_small = aps["ids_small"].unsqueeze(0).broadcast_to([P, NOH, B])
    program(nc, aps["ids"], ids_small, aps["small"], aps["row_of"],
            [aps["w_pair"][q] for q in range(NP)], [aps.get(f"tbl_{f}") for f in order],
            aps["w_top1"], aps["w_top2"], aps["w_top3"], aps["b_top1"], aps["b_top2"], aps["dense"],
            aps["ident"], aps["sel"], aps["sel_pair"], aps["sel_dense"], out.rearrange("b o -> o b"))
    return run_bass_kernel_spmd(nc, [arrays], core_ids=[0]).results[0]["y"]
```
